# Optimizing a Trainium2 kernel written in Bass

```python
import numpy as np
import jax
import jax.numpy as jnp

def _softmax(x, axis=-1):
    return jax.nn.softmax(x, axis=axis)

def _gelu(x):
    return jax.nn.gelu(x, approximate=True)

def _silu(x):
    return jax.nn.silu(x)

def _sigmoid(x):
    return jax.nn.sigmoid(x)

def _layernorm(x, axis=-1, eps=1e-05):
    m = jnp.mean(x, axis=axis, keepdims=True)
    v = jnp.var(x, axis=axis, keepdims=True)
    return (x - m) / jnp.sqrt(v + eps)

def _scatter_add(tgt, idx, src, axis=0):
    return tgt.at[idx].add(src)

def _segment_sum(src, seg, n):
    return jax.ops.segment_sum(src, seg, n)
kernel_name = 'mk_xattn_ffn_d1_seqx_r8_cc98d9'

def setup_inputs(seed: int=0):
    np.random.seed(seed)
    _w = jnp.asarray

    def _rec_inputs():
        import jax
        import jax.numpy as jnp
        _rk = jax.random.key(seed)
        x = 7.22e-05 + 1 * jax.random.normal(jax.random.fold_in(_rk, 1), (64, 64, 256), jnp.float32)
        _lenS = 64 - jax.random.randint(jax.random.fold_in(_rk, 7), (64,), 0, max(1, 64 // 4) + 1, jnp.int32)
        _lenS2 = 64 - jax.random.randint(jax.random.fold_in(_rk, 8), (64,), 0, max(1, 64 // 4) + 1, jnp.int32)
        _ctx_512P = jax.random.normal(jax.random.fold_in(_rk, 11), (64, 16, 64), jnp.float32)
        _ctx_512c = jax.random.dirichlet(jax.random.fold_in(_rk, 511), 0.3 * jnp.ones((16,), jnp.float32), (64, 64))
        _ctx_512t = jnp.einsum('bsk,bkd->bsd', _ctx_512c, _ctx_512P)
        _ctx_512t = _ctx_512t * jax.lax.rsqrt(jnp.mean(jnp.square(_ctx_512t)) + 1e-12) * 0.953939
        ctx_512 = -0.000514642 + 1.00011 * (_ctx_512t + 0.3 * jax.random.normal(jax.random.fold_in(_rk, 611), (64, 64, 64), jnp.float32))
        return (x, ctx_512)
    x, ctx_512 = _rec_inputs()

    def _L0_xattn_setup():
        import jax, jax.numpy as jnp
        import numpy as np
        B, S, H, NH, L = (2, 256, 256, 16, 64)
        HD = H // NH
        key = jax.random.key(seed)
        k1, k2, k3, k4, k5 = jax.random.split(key, 5)
        scale = 0.02
        return {'q': jax.random.normal(k1, (B, S, H), dtype=jnp.float32), 'latent_kv': jax.random.normal(k2, (B, S, L), dtype=jnp.float32), 'Wq': jax.random.normal(k3, (H, H), dtype=jnp.float32) * scale, 'Wkv_expand': jax.random.normal(k4, (2 * H, L), dtype=jnp.float32) * scale, 'Wout': jax.random.normal(k5, (H, H), dtype=jnp.float32) * scale}
    _L0_xattn_all = _L0_xattn_setup()
    _L0_xattn_in = {k: v for k, v in _L0_xattn_all.items() if k in ('Wq', 'Wkv_expand', 'Wout')}
    del _L0_xattn_all

    def _L0_ffn_setup():
        import jax, jax.numpy as jnp
        import numpy as np
        from jax import lax
        B, S, H = (1, 256, 256)
        E, I, TOP_K = (64, 64, 8)
        SHARED_I = 64
        key = jax.random.key(seed)
        ks = jax.random.split(key, 8)
        sc = 0.02
        return {'hidden_states': jax.random.normal(ks[0], (B, S, H), jnp.float32), 'router_w': jax.random.normal(ks[1], (E, H), jnp.float32) * sc, 'gate_up_proj': jax.random.normal(ks[2], (E, 2 * I, H), jnp.float32) * sc, 'down_proj': jax.random.normal(ks[3], (E, H, I), jnp.float32) * sc, 'shared_gate_w': jax.random.normal(ks[4], (SHARED_I, H), jnp.float32) * sc, 'shared_up_w': jax.random.normal(ks[5], (SHARED_I, H), jnp.float32) * sc, 'shared_down_w': jax.random.normal(ks[6], (H, SHARED_I), jnp.float32) * sc, 'shared_expert_gate_w': jax.random.normal(ks[7], (1, H), jnp.float32) * sc}
    _L0_ffn_all = _L0_ffn_setup()
    _L0_ffn_in = {k: v for k, v in _L0_ffn_all.items() if k in ('router_w', 'gate_up_proj', 'down_proj', 'shared_gate_w', 'shared_up_w', 'shared_down_w', 'shared_expert_gate_w')}
    del _L0_ffn_all
    return {'x': x, 'ctx_512': ctx_512, 'L0_xattn_Wq': _L0_xattn_in['Wq'], 'L0_xattn_Wkv_expand': _L0_xattn_in['Wkv_expand'], 'L0_xattn_Wout': _L0_xattn_in['Wout'], 'L0_ffn_router_w': _L0_ffn_in['router_w'], 'L0_ffn_gate_up_proj': _L0_ffn_in['gate_up_proj'], 'L0_ffn_down_proj': _L0_ffn_in['down_proj'], 'L0_ffn_shared_gate_w': _L0_ffn_in['shared_gate_w'], 'L0_ffn_shared_up_w': _L0_ffn_in['shared_up_w'], 'L0_ffn_shared_down_w': _L0_ffn_in['shared_down_w'], 'L0_ffn_shared_expert_gate_w': _L0_ffn_in['shared_expert_gate_w']}

def reference(x, ctx_512, L0_xattn_Wq, L0_xattn_Wkv_expand, L0_xattn_Wout, L0_ffn_router_w, L0_ffn_gate_up_proj, L0_ffn_down_proj, L0_ffn_shared_gate_w, L0_ffn_shared_up_w, L0_ffn_shared_down_w, L0_ffn_shared_expert_gate_w):
    import jax
    import jax.numpy as jnp

    def _L0_xattn_ref(q, latent_kv, Wq, Wkv_expand, Wout):
        import jax, jax.numpy as jnp
        import numpy as np
        B, S, H, NH, L = (2, 256, 256, 16, 64)
        HD = H // NH
        b, sq, _ = q.shape
        sk = latent_kv.shape[1]
        qp = q @ Wq.T
        kv = latent_kv @ Wkv_expand.T
        k, v = jnp.split(kv, 2, axis=-1)
        qh = qp.reshape(b, sq, NH, HD).transpose(0, 2, 1, 3)
        kh = k.reshape(b, sk, NH, HD).transpose(0, 2, 1, 3)
        vh = v.reshape(b, sk, NH, HD).transpose(0, 2, 1, 3)
        inv_sqrt_d = 1.0 / jnp.sqrt(jnp.float32(HD))
        scores = jnp.einsum('bhqd,bhkd->bhqk', qh, kh) * inv_sqrt_d
        causal = jnp.tril(jnp.ones((sq, sk), dtype=bool))
        scores = jnp.where(causal, scores, jnp.finfo(scores.dtype).min)
        attn = jax.nn.softmax(scores, axis=-1)
        out = jnp.einsum('bhqk,bhkd->bhqd', attn, vh)
        out = out.transpose(0, 2, 1, 3).reshape(b, sq, H)
        return out @ Wout.T

    def _L0_ffn_ref(hidden_states, router_w, gate_up_proj, down_proj, shared_gate_w, shared_up_w, shared_down_w, shared_expert_gate_w):
        import jax, jax.numpy as jnp
        import numpy as np
        from jax import lax
        B, S, H = (1, 256, 256)
        E, I, TOP_K = (64, 64, 8)
        SHARED_I = 64
        b, s, h_dim = hidden_states.shape
        h = hidden_states.reshape(-1, h_dim)
        T = h.shape[0]
        shared = jnp.dot(jax.nn.silu(jnp.dot(h, shared_gate_w.T)) * jnp.dot(h, shared_up_w.T), shared_down_w.T)
        shared = jax.nn.sigmoid(jnp.dot(h, shared_expert_gate_w.T)) * shared
        logits = jnp.dot(h, router_w.T)
        probs = jax.nn.softmax(logits.astype(jnp.float32), axis=-1)
        top_vals, top_idx = lax.top_k(probs, TOP_K)
        top_vals = top_vals / jnp.sum(top_vals, axis=-1, keepdims=True)
        top_vals = top_vals.astype(h.dtype)
        comb = jnp.zeros((T, E), h.dtype).at[jnp.arange(T)[:, None], top_idx].add(top_vals)

        def body(acc, xs):
            wgu, wd, w_e = xs
            g, u = jnp.split(jnp.dot(h, wgu.T), 2, axis=-1)
            eo = jnp.dot(jax.nn.silu(g) * u, wd.T)
            return (acc + eo * w_e[:, None], None)
        expert_out, _ = lax.scan(body, jnp.zeros_like(h), (gate_up_proj, down_proj, comb.T))
        return (expert_out + shared).reshape(b, s, h_dim)
    x = x + _L0_xattn_ref(_layernorm(x, axis=-1), ctx_512, L0_xattn_Wq, L0_xattn_Wkv_expand, L0_xattn_Wout)
    x = x + _L0_ffn_ref(_layernorm(x, axis=-1), L0_ffn_router_w, L0_ffn_gate_up_proj, L0_ffn_down_proj, L0_ffn_shared_gate_w, L0_ffn_shared_up_w, L0_ffn_shared_down_w, L0_ffn_shared_expert_gate_w)
    return x

_drawn_inputs = setup_inputs


def setup_inputs(seed=0):
    import zlib

    import numpy as np

    out = dict(_drawn_inputs(seed))
    spreads = {}
    factors = {'L0_xattn_Wq': 33.541,
     'L0_ffn_router_w': 8.0,
     'L0_ffn_gate_up_proj': 8.0,
     'L0_ffn_down_proj': 8.0,
     'L0_ffn_shared_gate_w': 8.0,
     'L0_ffn_shared_up_w': 8.0,
     'L0_ffn_shared_down_w': 8.0,
     'L0_ffn_shared_expert_gate_w': 8.0}
    for name, (base, spread) in spreads.items():
        noise = np.random.default_rng([zlib.crc32(name.encode()), seed]).standard_normal(out[name].shape)
        drawn = base * np.exp(spread * noise) if base else spread * noise
        out[name] = jnp.asarray(drawn.astype(out[name].dtype))
    for name, factor in factors.items():
        out[name] = (out[name] * factor).astype(out[name].dtype)
    return out
```

```python
from contextlib import ExitStack

import concourse.bass as bass
from concourse import mybir

F32 = mybir.dt.float32
BF16 = mybir.dt.bfloat16
I32 = mybir.dt.int32
U32 = mybir.dt.uint32
ALU = mybir.AluOpType
ACT = mybir.ActivationFunctionType
AX = mybir.AxisListType

P = 128
SEQ = 64
D = 256
KC = D // P
L = 64
NH, HD = 16, 16
HP = NH // 2
TOKENS = 64 * SEQ
NB = TOKENS // P
E, I, TOPK = 64, 64, 8
LN_EPS = 1e-5
SCORE_SCALE = HD ** -0.5
PVW = 2 * HD + 2
W8 = I + 1 + I + E
ROW = D + 2
HB = NB // 2
REGION = HB + 1
SPARE = E * REGION
TH = -(-(HB * TOPK + E - 1) // 8) * 8
TILES = 2 * TH
NOWHERE = 1 << 20
MASKED = -1e30
REMOVED = -3e38
C_IDENT, C_UPPER, C_CAUSAL, C_EXPERT, C_REGION = 0, P, 2 * P, 2 * P + 4 * SEQ, 2 * P + 4 * SEQ + E
C_WIDTH = C_REGION + E


def build(nc, x, ctxT, wq, wk, wv, wo, w8, sd, wgu, wd, consts, out):
    xf = x.rearrange("b s d -> (b s) d")
    of = out.rearrange("b s d -> (b s) d")
    dispatch = [nc.dram_tensor(f"dispatch{h}", [(SPARE + 1) * P, ROW], F32, kind="Internal").ap() for h in range(2)]
    results = nc.dram_tensor("results", [TOKENS * TOPK, D], F32, kind="Internal").ap()

    with ExitStack() as es:
        def sb(name, shape, dt=F32):
            return es.enter_context(nc.sbuf_tensor(name, shape, dt))

        def sem(name):
            return es.enter_context(nc.semaphore(name))

        ps = es.enter_context(nc.psum_tensor("ps", [P, 8, 512], F32))

        X = sb("X", [P, NB, D])
        WGU = sb("WGU", [P, KC, E, 2 * I])
        WD = sb("WD", [P, E, D])
        H2 = sb("H2", [P, 2 * TOPK * ROW])
        WQ = sb("WQ", [P, KC, D])
        WO = sb("WO", [P, KC, D])
        WE = sb("WE", [P, KC, W8])
        xh = sb("xh", [P, D])
        xhT = sb("xhT", [P, KC, P])
        qT = sb("qT", [P, KC, P])
        kM = sb("kM", [P, 2 * KC, P])
        VBD = sb("VBD", [P, 2, HP, PVW])
        SM = sb("SM", [P, 4, 4, SEQ])
        PT = sb("PT", [P, HP, P])
        attn = sb("attn", [P, HP, 2, HD])
        attnT = sb("attnT", [P, KC, P])
        h2T = sb("h2T", [P, KC, P])
        ident = sb("ident", [P, P])
        identb = sb("identb", [P, P], BF16)
        upperb = sb("upperb", [P, P], BF16)
        onesb = sb("onesb", [P, P], BF16)
        causalb = sb("causalb", [P, 4 * SEQ], BF16)
        expertno = sb("expertno", [P, E])
        regionrow = sb("regionrow", [P, E])
        places = sb("places", [P, TOPK], I32)
        junk = sb("junk", [P, TOPK, E], BF16)
        maskb = sb("maskb", [P, E], BF16)
        msum = sb("msum", [P, E], BF16)
        msum0 = sb("msum0", [P, E], BF16)
        small = sb("small", [P, 408])

        up = WD[L:P].rearrange("p e d -> p (e d)")
        WK = up[:, 0:512].rearrange("p (a m) -> p a m", a=2 * KC)
        WV = up[:, 512:768].rearrange("p (a m) -> p a m", a=2)
        CTX = up[:, 768:1024].rearrange("p (s t) -> p s t", s=2)
        SD = up[:, 1024:1280]
        hsT = up[:, 1280:1408]

        at = [0]

        def cut(n):
            at[0] += n
            return small[:, at[0] - n:at[0]]

        st1, st2 = cut(6), cut(6)
        mv1 = cut(4).rearrange("p (s c) -> p s c", s=2)
        mv2 = cut(2)
        ve1, ve2, rstd1, rstd2, half = cut(1), cut(1), cut(2), cut(1), cut(1)
        mx, rden = cut(NH), cut(NH)
        top, dtop, ew, idxf, posf = cut(8), cut(8), cut(8), cut(8), cut(8)
        wsum, rsum = cut(1), cut(1)
        idx = cut(8).bitcast(U32)
        posi = cut(16).bitcast(I32).rearrange("p (s k) -> p s k", s=2)
        eg, hs = cut(I + 1), cut(I)
        pose, rep = cut(E), cut(E)

        h2x = H2[:, :].rearrange("p (s k c) -> p s k c", s=2, k=TOPK)
        stage = SM[:, :, :, :].rearrange("p a b c -> p (a b c)")

        NS = 8
        xt = H2[:, 0:NS * ROW].rearrange("p (s c) -> p s c", s=NS)
        eo = H2[:, NS * ROW:NS * (ROW + D)].rearrange("p (s c) -> p s c", s=NS)
        xTs = PT[:, 0:4, :].rearrange("p (s k) t -> p s k t", s=2)
        smf = SM[:, :, :, :].rearrange("p a b c -> p (a b c)")
        gate = smf[:, 0:128].rearrange("p (s c) -> p s c", s=2)
        hid = smf[:, 128:256].rearrange("p (s c) -> p s c", s=2)
        hTs = smf[0:I, 256:512].rearrange("p (s c) -> p s c", s=2)
        padrow = sb("padrow", [1, 2, E], I32)
        padding = sb("padding", [P, ROW])
        cin = kM[0:E, 0, 0:8]
        cii = kM[0:E, 1, 0:8].bitcast(I32)
        colb = sb("colb", [E, 4], BF16)
        tilei = WQ[0:E, :, :].rearrange("p a b -> p (a b)")[:, 0:TH].bitcast(I32)
        tilef = WQ[0:E, :, :].rearrange("p a b -> p (a b)")[:, TH:2 * TH]
        rowf = [xh[0:1, 0:TH], xhT[0:1, :, :].rearrange("p a b -> p (a b)")[:, 0:TH]]
        geb = attn[0:E, :, :, :].rearrange("p a b c -> p (a b c)")[:, 0:TH].bitcast(BF16).rearrange(
            "p (h t) -> p h t", h=2)
        etab = WE[0:1, :, :].rearrange("p a b -> p (a b)")[:, 0:TILES].bitcast(I32)
        rtab = WO[0:1, :, :].rearrange("p a b -> p (a b)")[:, 0:TILES].bitcast(I32)

        res = WGU[:, :, :, :].rearrange("p k e m -> p (k e m)").rearrange("p (s k d) -> p s k d", s=NS, k=TOPK)

        S_ps = ps[:, 0:4, 0:256].rearrange("p r (a t) -> p r a t", a=4)
        k_ps = ps[:, 0, :].rearrange("p (a t) -> p a t", a=2 * KC)
        wo_ps = ps[:, 1, 0:D]
        q_ps = ps[:, 2, 0:D].rearrange("p (c t) -> p c t", c=KC)
        xT_ps = ps[:, 3, 0:D].rearrange("p (c t) -> p c t", c=KC)
        hsT_ps = ps[0:I, 3, 0:P]
        v_ps = ps[:, 4, 0:D].rearrange("p (b m) -> p b m", b=2)
        aT_ps = ps[:, 5, 0:D].rearrange("p (c t) -> p c t", c=KC)
        pv_ps = ps[:, 5, 0:HP * PVW].rearrange("p (h c) -> p h c", h=HP)
        PT_ps = [ps[:, b, :].rearrange("p (j t) -> p j t", j=4) for b in (5, 7)]
        pre_ps = ps[:, 6, 0:E]
        cnt_ps = ps[0:1, 6, E:2 * E]
        sd_ps = ps[:, 6, 0:D]
        h2T_ps = ps[:, 7, 0:D].rearrange("p (c t) -> p c t", c=KC)
        g8_ps = ps[:, 7, 0:W8]
        g_ps, sg_ps, u_ps, lg_ps = (g8_ps[:, 0:I], g8_ps[:, I:I + 1], g8_ps[:, I + 1:2 * I + 1], g8_ps[:, 2 * I + 1:W8])

        consts_in = sem("consts_in")
        weights_in = sem("weights_in")
        experts_in = sem("experts_in")
        block_in = [sem("block_in0"), sem("block_in1")]
        zeroed = sem("zeroed")
        SETUP = 11
        setup = sem("setup")
        places_made = sem("places_made")
        (stats1_done, var1_ready, eps1_done, rstd1_ready, xh_ready, xhT_made, xhT_ready, k_made, k_ready, v_made,
         v_ready, q_made, q_ready, s_made, mx_ready, sm_ready, p_ready, pt_made, pt_ready, pv_made, rden_ready,
         an_ready, attnT_made, attnT_ready, wo_made, x1_ready, stats2_done, var2_ready, eps2_done, rstd2_ready,
         h2_ready, h2c_ready, h2T_made, h2T_ready, g8_made, top_ready, rep_ready, dtop_ready, mask_ready, idx_ready,
         idxf_ready, ew_ready, rsum_ready, w_ready, eg_ready, egp_ready, egr_ready, hsg_ready, hs_ready, pre_made,
         hsT_made, hsT_ready, sd_made, resid_ready, pose_ready, posf_ready, pos_ready, msum_ready, place_ready) = (
            sem(n) for n in (
                "stats1_done var1_ready eps1_done rstd1_ready xh_ready xhT_made xhT_ready k_made k_ready v_made "
                "v_ready q_made q_ready s_made mx_ready sm_ready p_ready pt_made pt_ready pv_made rden_ready "
                "an_ready attnT_made attnT_ready wo_made x1_ready stats2_done var2_ready eps2_done rstd2_ready "
                "h2_ready h2c_ready h2T_made h2T_ready g8_made top_ready rep_ready dtop_ready mask_ready idx_ready "
                "idxf_ready ew_ready rsum_ready w_ready eg_ready egp_ready egr_ready hsg_ready hs_ready pre_made "
                "hsT_made hsT_ready sd_made resid_ready pose_ready posf_ready pos_ready msum_ready place_ready").split())
        dispatched = [sem("dispatched0"), sem("dispatched1")]
        counts_made, tab_step, tab_ready, ends_made, rows_made, tileno_ready = (
            sem(n) for n in "counts_made tab_step tab_ready ends_made rows_made tileno_ready".split())
        spare_in, pads_in = sem("spare_in"), [sem("pads_in0"), sem("pads_in1")]
        halved, half_counts, padrow_ready, padding_ready = (
            sem(n) for n in "halved half_counts padrow_ready padding_ready".split())
        xt_in = [sem(f"xt_in{s}") for s in range(NS)]
        scattered = [sem(f"scattered{s}") for s in range(NS)]
        xT_made, xT_ready, gu_made, gate_ready, hid_ready, hT_made, hT_ready, eo_made, eo_ready = (
            sem(n) for n in "xT_made xT_ready gu_made gate_ready hid_ready hT_made hT_ready eo_made eo_ready".split())
        res_in = [sem(f"res_in{s}") for s in range(NS)]
        red_done, out_ready = sem("red_done"), sem("out_ready")
        out_in = [sem("out_in0"), sem("out_in1")]

        block = es.enter_context(nc.Block())

        def steps(eng, step, second=None):
            for i in range(3):
                step(i, i % 2)
            with eng.Fori(3, HB + 1 - (2 - 1), 2) as i:
                step(i, 1)
                step(i + 1, 0)
            for i in range(HB + 1, HB + 5):
                if i == HB + 3 and second:
                    step = second
                step(i, i % 2)
            with eng.Fori(HB + 5, NB - 3 - (2 - 1), 2) as i:
                step(i, 1)
                step(i + 1, 0)
            for i in range(NB - 3, NB + 3):
                step(i, i % 2)

        passed = {}

        def apart(eng):
            if eng not in passed:
                passed[eng] = sem(f"passed{len(passed)}")
            eng.sem_inc(passed[eng], 1)

        def there(i):
            return not isinstance(i, int) or 0 <= i < NB

        def tile_steps(eng, step):
            for j in range(8):
                step(j, j)
            with eng.Fori(8, TILES - (8 - 1), 8) as j:
                for u in range(8):
                    step(j + u, u)
            for j in range(TILES, TILES + 4):
                step(j, j)

        def tile_there(j):
            return not isinstance(j, int) or 0 <= j < TILES

        def block_count(i, s):
            return (i - s) * 16 + 32

        def dispatched_count(i, s):
            return (i - s) * (8 * TOPK)

        def slot_count(j, s):
            return (j - s) * 2 + 16

        @block.sync
        def _(sp):
            sp.dma_start(stage[:, 0:C_WIDTH], consts).then_inc(consts_in, 16)

            def load(i, s):
                if not there(i):
                    return
                if not (isinstance(i, int) and i < 2):
                    sp.wait_ge(v_made, i - 1)
                sp.dma_start(X[:, i, :], xf.rearrange("(n p) d -> n p d", p=P)[i]).then_inc(block_in[s], 16)
                sp.dma_start(CTX[:, s, :], ctxT[i]).then_inc(block_in[s], 16)

            load(0, 0)
            sp.dma_start(WQ[:, :, :], wq).then_inc(weights_in, 16)
            sp.dma_start(WK, wk).then_inc(weights_in, 16)
            sp.dma_start(WV, wv).then_inc(weights_in, 16)
            load(1, 1)
            sp.dma_start(WO[:, :, :], wo).then_inc(weights_in, 16)
            sp.dma_start(WE[:, :, :], w8).then_inc(weights_in, 16)
            sp.dma_start(SD, sd).then_inc(weights_in, 16)
            with sp.Fori(2, HB + 6 - (2 - 1), 2) as i:
                load(i, 0)
                load(i + 1, 1)

            def pad(h, e):
                r = sp.value_load(padrow[0:1, h, bass.ds(e, 1)], min_val=0, max_val=SPARE * P)
                sp.dma_start(dispatch[h][bass.ds(r, P), :], padding[:, :]).then_inc(pads_in[h], 16)

            sp.wait_ge(padding_ready, 2)
            for h in range(2):
                sp.dma_start(dispatch[h][SPARE * P:(SPARE + 1) * P, :], padding[:, :]).then_inc(spare_in, 16)
            sp.wait_ge(padrow_ready, 1)
            with sp.Fori(0, E) as e:
                pad(0, e)
            with sp.Fori(HB + 6, NB - (2 - 1), 2) as i:
                load(i, 0)
                load(i + 1, 1)

            tiles_of = [d.rearrange("(t p) c -> t p c", p=P) for d in dispatch]

            def load_tile(h, j, s):
                sp.wait_ge(scattered[s], j * 2)
                r = sp.value_load(rtab[0:1, bass.ds(j + s, 1)], min_val=0, max_val=SPARE)
                sp.dma_start(xt[:, s, :], tiles_of[h][r]).then_inc(xt_in[s], 16)

            sp.wait_ge(pads_in[0], 16 * E)
            sp.wait_ge(spare_in, 32)
            for s in range(2):
                sp.wait_ge(dispatched[s], NB // 2 * 16 * TOPK)
            sp.wait_ge(padrow_ready, 2)
            sp.wait_ge(tab_ready, 1)
            with sp.Fori(0, E * 2 - (NS - 1), NS) as j:
                for s in range(NS):
                    load_tile(0, j, s)
                for e in range(4):
                    pad(1, sp.snap(j // 2) + e)
            with sp.Fori(E * 2, TH - (NS - 1), NS) as j:
                for s in range(NS):
                    load_tile(0, j, s)
            sp.wait_ge(pads_in[1], 16 * E)
            with sp.Fori(TH, TILES - (NS - 1), NS) as j:
                for s in range(NS):
                    load_tile(1, j, s)

            for s in range(NS):
                sp.wait_ge(scattered[s], 16 * (TILES // NS))
            sp.wait_ge(gu_made, TILES)
            res_of = results.rearrange("(n p k) d -> n p k d", p=P, k=TOPK)
            for s in range(NS):
                sp.dma_start(res[:, s, :, :], res_of[s]).then_inc(res_in[s], 16)
            with sp.Fori(NS, NB - (NS - 1), NS) as i:
                for s in range(NS):
                    sp.wait_ge(red_done, i + (s + 1 - NS))
                    sp.dma_start(res[:, s, :, :], res_of[i + s]).then_inc(res_in[s], 16)

        @block.tensor
        def _(pe):
            pe.wait_ge(setup, SETUP)
            pe.wait_ge(weights_in, 16 * 6)

            def transpose_xh(i):
                if there(i):
                    pe.wait_ge(xh_ready, i + 1)
                    pe.wait_ge(sm_ready, i)
                    for c in range(KC):
                        t = pe.transpose(xT_ps[:, c, :], xh[:, c * P:(c + 1) * P], ident[:, :])
                    t.then_inc(xhT_made, 1)

            def project_k(i, s):
                if there(i):
                    pe.wait_ge(block_in[s], block_count(i, s))
                    for a in range(2 * KC):
                        t = pe.matmul(k_ps[:, a, :], WK[:, a, :], CTX[:, s, :], start=True, stop=True)
                    t.then_inc(k_made, 1)

            def project_v(i, s):
                if there(i):
                    pe.wait_ge(v_ready, i)
                    apart(pe)
                    for b in range(2):
                        for a in range(2):
                            t = pe.matmul(v_ps[a * SEQ:(a + 1) * SEQ, b, :], CTX[:, s, b * SEQ:(b + 1) * SEQ],
                                          WV[:, a, :], start=True, stop=True)
                    t.then_inc(v_made, 1)

            def project_q(i):
                if there(i):
                    pe.wait_ge(xhT_ready, i + 1)
                    for c in range(KC):
                        for kc in range(KC):
                            t = pe.matmul(q_ps[:, c, :], WQ[:, kc, c * P:(c + 1) * P], xhT[:, kc, :],
                                          start=(kc == 0), stop=(kc == KC - 1))
                    t.then_inc(q_made, 1)

            def scores(i):
                if there(i):
                    pe.wait_ge(q_ready, i + 1)
                    pe.wait_ge(k_ready, i + 1)
                    if not (isinstance(i, int) and i < 2):
                        pe.wait_ge(x1_ready, i - 1)
                    if not (isinstance(i, int) and i < 3):
                        pe.wait_ge(hsT_ready, i - 2)
                    for r in range(4):
                        pe.matmul(ps[:, r, 0:256], identb[:, :], causalb[:, :], start=True, stop=False,
                                  skip_group_check=True)
                    for b in range(2):
                        for c in range(KC):
                            for r in range(4):
                                rows = slice(32 * r, 32 * r + 32)
                                seq = slice(b * SEQ, (b + 1) * SEQ)
                                t = pe.matmul(S_ps[seq, r, 2 * c:2 * c + 2, :], qT[rows, c, seq],
                                              kM[rows, 2 * c:2 * c + 2, seq], start=False, stop=True,
                                              skip_group_check=True)
                    t.then_inc(s_made, 1)

            def transpose_p(i):
                if there(i):
                    pe.wait_ge(p_ready, i + 1)
                    for h in range(2):
                        if h == 0:
                            pe.wait_ge(attnT_ready, i)
                        elif not (isinstance(i, int) and i < 2):
                            pe.wait_ge(hs_ready, i - 1)
                            pe.wait_ge(idx_ready, i - 1)
                        for j in range(4):
                            r, c = (4 * h + j) // 2, j % 2
                            t = pe.transpose(PT_ps[h][:, j, :], SM[:, r, 2 * c:2 * c + 2, :], ident[:, :])
                        t.then_inc(pt_made, 1)

            def times_v(i):
                if there(i):
                    pe.wait_ge(pt_ready, i * 2 + 2)
                    pe.wait_ge(v_ready, i + 1)
                    for b in range(2):
                        seq = slice(b * SEQ, (b + 1) * SEQ)
                        for t_ in range(HP):
                            r, c = t_ // 2, t_ % 2
                            hp = 4 * c + r
                            t = pe.matmul(pv_ps[seq, hp, :], PT[:, t_, seq], VBD[:, b, hp, :], start=True, stop=True)
                    t.then_inc(pv_made, 1)

            def transpose_attn(i):
                if there(i):
                    pe.wait_ge(an_ready, i + 1)
                    for c in range(KC):
                        t = pe.transpose(aT_ps[:, c, :], attn[:, 4 * c:4 * c + 4, :, :], ident[:, :])
                    t.then_inc(attnT_made, 1)

            def project_out(i):
                if there(i):
                    pe.wait_ge(attnT_ready, i + 1)
                    pe.wait_ge(sm_ready, min(i + 2, NB) if isinstance(i, int) else i + 2)
                    for kc in range(KC):
                        t = pe.matmul(wo_ps, attnT[:, kc, :], WO[:, kc, :], start=(kc == 0), stop=(kc == KC - 1))
                    t.then_inc(wo_made, 1)

            def transpose_h2(i, s):
                if there(i):
                    pe.wait_ge(h2_ready, i + 1)
                    pe.wait_ge(pt_ready, min(i * 2 + 4, NB * 2) if isinstance(i, int) else i * 2 + 4)
                    for c in range(KC):
                        t = pe.transpose(h2T_ps[:, c, :], h2x[:, s, 0, c * P:(c + 1) * P], ident[:, :])
                    t.then_inc(h2T_made, 1)

            def shared_and_router(i):
                if there(i):
                    pe.wait_ge(h2T_ready, i + 1)
                    for kc in range(KC):
                        t = pe.matmul(g8_ps, h2T[:, kc, :], WE[:, kc, :], start=(kc == 0), stop=(kc == KC - 1))
                    t.then_inc(g8_made, 1)

            def prefix(i):
                if there(i):
                    pe.wait_ge(resid_ready, i)
                    if isinstance(i, int) and i == HB:
                        pe.wait_ge(halved, 2)
                        pe.matmul(cnt_ps, onesb[:, 0:1], msum0[:, :], start=True, stop=True).then_inc(half_counts, 1)
                    pe.wait_ge(mask_ready, i + 1)
                    pe.wait_ge(msum_ready, i)
                    pe.matmul(pre_ps, upperb[:, :], maskb[:, :], start=True, stop=False)
                    pe.matmul(pre_ps, onesb[:, :], msum[:, :], start=False, stop=True).then_inc(pre_made, 1)
                    pe.wait_ge(hs_ready, i + 1)
                    pe.wait_ge(xhT_ready, min(i + 4, NB) if isinstance(i, int) else i + 4)
                    apart(pe)
                    pe.transpose(hsT_ps, hs, ident[:, :]).then_inc(hsT_made, 1)

            def shared_down(i):
                if there(i):
                    pe.wait_ge(hsT_ready, i + 1)
                    pe.wait_ge(pose_ready, i + 1)
                    pe.matmul(sd_ps, hsT, SD, start=True, stop=True).then_inc(sd_made, 1)

            def step(i, s):
                transpose_xh(i)
                project_k(i, s)
                project_v(i, s)
                transpose_attn(i - 2)
                project_q(i)
                project_out(i - 2)
                prefix(i - 3)
                transpose_p(i - 1)
                scores(i)
                shared_down(i - 3)
                transpose_h2(i - 2, s)
                times_v(i - 1)
                shared_and_router(i - 2)

            steps(pe, step)

            pe.wait_ge(msum_ready, NB)
            pe.wait_ge(resid_ready, NB)
            pe.matmul(ps[0:E, 0, 0:1], msum0[:, :], onesb[:, 0:1], start=True, stop=True)
            pe.matmul(ps[0:E, 0, 1:2], msum[:, :], onesb[:, 0:1], start=True, stop=True)
            pe.matmul(ps[0:1, 1, 0:E], onesb[:, 0:1], msum[:, :], start=True, stop=True).then_inc(counts_made, 1)
            pe.wait_ge(tab_step, 4)
            pe.matmul(ps[0:E, 2, 0:2], upperb[0:E, 0:E], colb[:, 0:2], start=True, stop=False)
            pe.matmul(ps[0:E, 2, 0:2], identb[0:E, 0:E], colb[:, 0:2], start=False, stop=True).then_inc(ends_made, 1)
            pe.wait_ge(tab_step, 7)
            pe.matmul(ps[0:1, 3, 0:TILES], onesb[0:E, 0:1], geb[:, :, :], start=True, stop=True)
            for h in range(2):
                t = pe.matmul(ps[0:1, 4, h * TH:(h + 1) * TH], colb[:, 2 + h:3 + h], geb[:, h, :], start=True, stop=True)
            t.then_inc(rows_made, 1)

            pe.wait_ge(experts_in, 32)
            pe.wait_ge(tab_ready, 1)

            def expert_of(j):
                return pe.value_load(etab[0:1, bass.ds(j, 1)], min_val=0, max_val=E - 1)

            def tile_transpose(j, u):
                if tile_there(j):
                    pe.wait_ge(xt_in[u % NS], slot_count(j, u % NS))
                    if not (isinstance(j, int) and j < 2):
                        pe.wait_ge(xT_ready, j - 1)
                    for c in range(KC):
                        t = pe.transpose(ps[:, u % 2, c * P:(c + 1) * P], xt[:, u % NS, c * P:(c + 1) * P], ident[:, :])
                    t.then_inc(xT_made, 1)

            def tile_gate_up(j, u):
                if tile_there(j):
                    e = expert_of(j)
                    pe.wait_ge(xT_ready, j + 1)
                    if not (isinstance(j, int) and j < 2):
                        pe.wait_ge(hid_ready, j - 1)
                    for kc in range(KC):
                        t = pe.matmul(ps[:, 2 + u % 2, 0:2 * I], xTs[:, u % 2, kc, :], WGU[:, kc, e, :],
                                      start=(kc == 0), stop=(kc == KC - 1))
                    t.then_inc(gu_made, 1)

            def tile_transpose_hidden(j, u):
                if tile_there(j):
                    pe.wait_ge(hid_ready, j + 1)
                    if not (isinstance(j, int) and j < 2):
                        pe.wait_ge(hT_ready, j - 1)
                    apart(pe)
                    pe.transpose(ps[0:I, 4 + u % 2, 0:P], hid[:, u % 2, :], ident[:, :]).then_inc(hT_made, 1)

            def tile_down(j, u):
                if tile_there(j):
                    e = expert_of(j)
                    pe.wait_ge(hT_ready, j + 1)
                    if not (isinstance(j, int) and j < 2):
                        pe.wait_ge(eo_ready, j - 1)
                    pe.matmul(ps[:, 6 + u % 2, 0:D], hTs[:, u % 2, :], WD[0:I, e, :], start=True,
                              stop=True).then_inc(eo_made, 1)

            def tile_step(j, u):
                tile_transpose(j, u)
                tile_gate_up(j - 1, u + 7)
                tile_transpose_hidden(j - 3, u + 5)
                tile_down(j - 4, u + 4)

            tile_steps(pe, tile_step)

        @block.scalar
        def _(act):
            act.dma_start(WGU[:, :, :, :], wgu).then_inc(experts_in, 16)
            act.dma_start(WD[0:I, :, :], wd).then_inc(experts_in, 16)
            act.wait_ge(setup, SETUP)

            def gates(i):
                if there(i):
                    act.wait_ge(g8_made, i + 1)
                    act.wait_ge(hs_ready, i)
                    act.activation(eg, g8_ps[:, 0:I + 1], ACT.Exp, scale=-1.0).then_inc(eg_ready, 1)

            def copy_xhT(i):
                if there(i):
                    act.wait_ge(xhT_made, i + 1)
                    act.wait_ge(q_made, i)
                    act.copy(xhT[:, :, :], xT_ps).then_inc(xhT_ready, 1)

            def copy_k(i):
                if there(i):
                    act.wait_ge(k_made, i + 1)
                    act.wait_ge(s_made, i)
                    act.copy(kM[:, :, :], k_ps).then_inc(k_ready, 1)

            def copy_v(i):
                if there(i):
                    act.wait_ge(v_made, i + 1)
                    act.wait_ge(pv_made, i)
                    for a in range(2):
                        half_ = slice(a * SEQ, (a + 1) * SEQ)
                        for b in range(2):
                            t = act.copy(VBD[half_, b, :, a * HD:(a + 1) * HD],
                                         v_ps[half_, b, :].rearrange("p (h d) -> p h d", h=HP))
                    t.then_inc(v_ready, 1)

            def copy_attnT(i):
                if there(i):
                    act.wait_ge(attnT_made, i + 1)
                    act.wait_ge(wo_made, i)
                    act.copy(attnT[:, :, :], aT_ps).then_inc(attnT_ready, 1)

            def copy_q(i):
                if there(i):
                    act.wait_ge(q_made, i + 1)
                    act.copy(qT[:, :, :], q_ps).then_inc(q_ready, 1)

            def choice_weights(i):
                if there(i):
                    act.wait_ge(dtop_ready, i + 1)
                    act.wait_ge(w_ready, i)
                    act.activation(ew, dtop, ACT.Exp, accum_out=wsum).then_inc(ew_ready, 1)

            def copy_hsT(i):
                if there(i):
                    act.wait_ge(hsT_made, i + 1)
                    act.wait_ge(sd_made, i)
                    act.copy(hsT, hsT_ps).then_inc(hsT_ready, 1)

            def copy_p(i):
                if there(i):
                    for h in range(2):
                        act.wait_ge(pt_made, i * 2 + 1 + h)
                        if h == 0:
                            act.wait_ge(pv_made, i)
                        act.copy(PT[:, 4 * h:4 * h + 4, :], PT_ps[h]).then_inc(pt_ready, 1)

            def copy_h2T(i):
                if there(i):
                    act.wait_ge(h2T_made, i + 1)
                    act.wait_ge(g8_made, i)
                    act.copy(h2T[:, :, :], h2T_ps).then_inc(h2T_ready, 1)

            def exponentials(i):
                if there(i):
                    act.wait_ge(sm_ready, i + 1)
                    act.activation(SM[:, :, :, :], SM[:, :, :, :], ACT.Exp, scale=SCORE_SCALE).then_inc(p_ready, 1)

            def step(i, s):
                gates(i - 3)
                copy_xhT(i)
                copy_k(i)
                copy_v(i - 1)
                copy_attnT(i - 2)
                copy_q(i)
                choice_weights(i - 3)
                copy_hsT(i - 3)
                copy_p(i - 1)
                copy_h2T(i - 2)
                exponentials(i)

            steps(act, step)

            def tile_gate(j, u):
                if tile_there(j):
                    act.wait_ge(gu_made, j + 1)
                    if not (isinstance(j, int) and j < 2):
                        act.wait_ge(hid_ready, j - 1)
                    act.activation(gate[:, u % 2, :], ps[:, 2 + u % 2, 0:I], ACT.Silu).then_inc(gate_ready, 1)

            def tile_result(j, u):
                if tile_there(j):
                    act.wait_ge(eo_made, j + 1)
                    act.wait_ge(scattered[u % NS], slot_count(j, u % NS) - 16)
                    act.copy(eo[:, u % NS, :], ps[:, 6 + u % 2, 0:D]).then_inc(eo_ready, 1)

            def tile_step(j, u):
                tile_gate(j - 1, u + 7)
                tile_result(j - 4, u + 4)

            tile_steps(act, tile_step)

            out_of = of.rearrange("(n p) d -> n p d", p=P)
            with act.Fori(0, NB - (2 - 1), 2) as i:
                for s in range(2):
                    act.wait_ge(out_ready, i + (s + 1))
                    act.dma_start(out_of[i + s], X[:, i + s, :]).then_inc(out_in[s], 16)
            for s in range(2):
                act.wait_ge(out_in[s], 16 * (NB // 2))

        @block.gpsimd
        def _(pool):
            pool.iota(places[:, :], [[1, TOPK]], base=0, channel_multiplier=TOPK).then_inc(places_made, 1)
            pool.wait_ge(setup, SETUP)

            def rstd_1(i, s):
                if there(i):
                    pool.wait_ge(var1_ready, i + 1)
                    pool.wait_ge(rstd1_ready, i)
                    apart(pool)
                    pool.tensor_scalar(ve1, mv1[:, s, 1:2], LN_EPS, None, ALU.add).then_inc(eps1_done, 1)
                    pool.wait_ge(eps1_done, i + 1)
                    pool.tensor_tensor(rstd1[:, s:s + 1], ve1, half, ALU.pow).then_inc(rstd1_ready, 1)

            def rstd_2(i):
                if there(i):
                    pool.wait_ge(var2_ready, i + 1)
                    pool.wait_ge(rstd2_ready, i)
                    apart(pool)
                    pool.tensor_scalar(ve2, mv2[:, 1:2], LN_EPS, None, ALU.add).then_inc(eps2_done, 1)
                    pool.wait_ge(eps2_done, i + 1)
                    pool.tensor_tensor(rstd2, ve2, half, ALU.pow).then_inc(rstd2_ready, 1)

            def scatter_rows(i, s, h):
                if there(i):
                    pool.wait_ge(dispatched[s], dispatched_count(i, s))
                    pool.wait_ge(places_made, i + 1)
                    apart(pool)
                    pool.tensor_copy(h2x[:, s, :, D + 1].bitcast(I32), places[:, :]).then_inc(place_ready, 1)
                    pool.wait_ge(place_ready, i + 1)
                    apart(pool)
                    pool.tensor_scalar(places[:, :], places[:, :], float(P * TOPK), None, ALU.add).then_inc(places_made, 1)
                    pool.wait_ge(h2c_ready, i + 1)
                    pool.wait_ge(w_ready, i + 1)
                    pool.wait_ge(pos_ready, i + 1)
                    apart(pool)
                    for k in range(TOPK):
                        pool.indirect_dma_start(dispatch[h], bass.IndirectOffsetOnAxis(posi[:, s, k:k + 1], 0),
                                                h2x[:, s, k, :], None).then_inc(dispatched[s], 16)

            def step_of(h):
                def step(i, s):
                    rstd_2(i - 2)
                    scatter_rows(i - 3, 1 - s, h)
                    rstd_1(i + 2, s)
                return step

            pool.wait_ge(places_made, 1)
            rstd_1(0, 0)
            rstd_1(1, 1)
            first, second = step_of(0), step_of(1)
            steps(pool, first, second)

            pool.wait_ge(q_made, NB)
            pool.iota(tilei, [[1, TH]], base=0, channel_multiplier=0).then_inc(tileno_ready, 1)

            with pool.Fori(0, TILES - (NS - 1), NS) as j:
                for s in range(NS):
                    pool.wait_ge(eo_ready, j + (s + 1))
                    apart(pool)
                    pool.indirect_dma_start(results, bass.IndirectOffsetOnAxis(xt[:, s, D + 1:D + 2].bitcast(I32), 0),
                                            eo[:, s, :], None, bounds_check=TOKENS * TOPK - 1,
                                            oob_is_err=False).then_inc(scattered[s], 16)

        @block.vector
        def _(dve):
            dve.memset(padding[:, 0:D + 1], 0.0).then_inc(padding_ready, 1)
            dve.memset(padding[:, D + 1:D + 2].bitcast(I32), NOWHERE).then_inc(padding_ready, 1)
            dve.memset(VBD[:, :, :, :], 0.0).then_inc(zeroed, 1)
            dve.memset(half, -0.5).then_inc(setup, 1)
            dve.memset(onesb[:, :], 1.0).then_inc(setup, 1)
            dve.memset(msum[:, :], 0.0).then_inc(setup, 1)
            dve.wait_ge(zeroed, 1)
            dve.memset(VBD[0:SEQ, :, :, 2 * HD:2 * HD + 1], 1.0).then_inc(setup, 1)
            dve.memset(VBD[SEQ:P, :, :, 2 * HD + 1:PVW], 1.0).then_inc(setup, 1)
            dve.wait_ge(consts_in, 16)
            dve.tensor_copy(ident[:, :], stage[:, C_IDENT:C_IDENT + P]).then_inc(setup, 1)
            dve.tensor_copy(identb[:, :], stage[:, C_IDENT:C_IDENT + P]).then_inc(setup, 1)
            dve.tensor_copy(upperb[:, :], stage[:, C_UPPER:C_UPPER + P]).then_inc(setup, 1)
            dve.tensor_copy(causalb[:, :], stage[:, C_CAUSAL:C_CAUSAL + 4 * SEQ]).then_inc(setup, 1)
            dve.tensor_copy(expertno[:, :], stage[:, C_EXPERT:C_EXPERT + E]).then_inc(setup, 1)
            dve.tensor_copy(regionrow[:, :], stage[:, C_REGION:C_REGION + E]).then_inc(setup, 1)
            dve.wait_ge(setup, SETUP)

            def stats_1(i, s):
                if there(i):
                    dve.wait_ge(block_in[s], block_count(i, s))
                    dve.wait_ge(var1_ready, i)
                    if not (isinstance(i, int) and i < 2):
                        dve.wait_ge(xh_ready, i - 1)
                    apart(dve)
                    dve.bn_stats(st1, X[:, i, :]).then_inc(stats1_done, 1)
                    dve.wait_ge(stats1_done, i + 1)
                    apart(dve)
                    dve.bn_aggr(mv1[:, s, :], st1).then_inc(var1_ready, 1)

            def normalise_1(i, s):
                if there(i):
                    dve.wait_ge(rstd1_ready, i + 1)
                    dve.wait_ge(xhT_made, i)
                    dve.tensor_scalar(xh[:, :], X[:, i, :], mv1[:, s, 0:1], rstd1[:, s:s + 1], ALU.subtract,
                                      ALU.mult).then_inc(xh_ready, 1)

            def row_max(i):
                if there(i):
                    dve.wait_ge(s_made, i + 1)
                    dve.tensor_reduce(mx.rearrange("p (r a) -> p r a", r=4), S_ps, AX.X, ALU.max).then_inc(mx_ready, 1)
                    dve.wait_ge(mx_ready, i + 1)
                    dve.wait_ge(pt_made, i * 2)
                    dve.tensor_tensor(SM[:, :, :, :], S_ps,
                                      mx.rearrange("p (r a) -> p r a", r=4).unsqueeze(3).broadcast_to([P, 4, 4, SEQ]),
                                      ALU.subtract).then_inc(sm_ready, 1)

            def divide(i):
                if there(i):
                    dve.wait_ge(pv_made, i + 1)
                    rd = rden.rearrange("p (h a) -> p h a", h=HP)
                    dve.reciprocal(rd, pv_ps[:, :, 2 * HD:PVW]).then_inc(rden_ready, 1)
                    dve.wait_ge(rden_ready, i + 1)
                    dve.wait_ge(attnT_made, i)
                    dve.tensor_tensor(attn[:, :, :, :], pv_ps[:, :, 0:2 * HD].rearrange("p h (a d) -> p h a d", a=2),
                                      rd.unsqueeze(3).broadcast_to([P, HP, 2, HD]), ALU.mult).then_inc(an_ready, 1)

            def route(i):
                if there(i):
                    dve.wait_ge(eg_ready, i + 1)
                    apart(dve)
                    dve.max(top, lg_ps).then_inc(top_ready, 1)
                    dve.wait_ge(top_ready, i + 1)
                    apart(dve)
                    dve.match_replace(rep, top, lg_ps, REMOVED).then_inc(rep_ready, 1)
                    dve.tensor_scalar(dtop, top, top[:, 0:1], None, ALU.subtract).then_inc(dtop_ready, 1)
                    dve.wait_ge(rep_ready, i + 1)
                    dve.wait_ge(pre_made, i)
                    dve.tensor_tensor(maskb[:, :], rep, lg_ps, ALU.not_equal).then_inc(mask_ready, 1)
                    dve.max_index(idx, top, lg_ps).then_inc(idx_ready, 1)
                    dve.wait_ge(idx_ready, i + 1)
                    dve.tensor_copy(idxf, idx).then_inc(idxf_ready, 1)

            def shared_hidden(i):
                if there(i):
                    dve.wait_ge(eg_ready, i + 1)
                    dve.tensor_scalar(eg, eg, 1.0, None, ALU.add).then_inc(egp_ready, 1)
                    dve.wait_ge(egp_ready, i + 1)
                    dve.reciprocal(eg, eg).then_inc(egr_ready, 1)
                    dve.wait_ge(egr_ready, i + 1)
                    dve.wait_ge(hsT_made, i)
                    dve.scalar_tensor_tensor(hs, eg[:, 0:I], eg[:, I:I + 1], g_ps, ALU.mult,
                                             ALU.mult).then_inc(hsg_ready, 1)
                    dve.wait_ge(hsg_ready, i + 1)
                    dve.tensor_tensor(hs, hs, u_ps, ALU.mult).then_inc(hs_ready, 1)

            def add_attention(i):
                if there(i):
                    dve.wait_ge(wo_made, i + 1)
                    dve.tensor_tensor(X[:, i, :], X[:, i, :], wo_ps, ALU.add).then_inc(x1_ready, 1)
                    dve.wait_ge(x1_ready, i + 1)
                    apart(dve)
                    dve.bn_stats(st2, X[:, i, :]).then_inc(stats2_done, 1)
                    dve.wait_ge(stats2_done, i + 1)
                    apart(dve)
                    dve.bn_aggr(mv2, st2).then_inc(var2_ready, 1)

            def weigh(i, s):
                if there(i):
                    dve.wait_ge(ew_ready, i + 1)
                    dve.reciprocal(rsum, wsum).then_inc(rsum_ready, 1)
                    dve.wait_ge(rsum_ready, i + 1)
                    dve.tensor_scalar(h2x[:, s, :, D], ew, rsum, None, ALU.mult).then_inc(w_ready, 1)

            def place(i, s):
                if there(i):
                    dve.wait_ge(pre_made, i + 1)
                    if isinstance(i, int) and i == HB:
                        dve.wait_ge(half_counts, 1)
                        dve.tensor_tensor(padrow[:, 0, :], cnt_ps, regionrow[0:1, :], ALU.add).then_inc(padrow_ready, 1)
                    dve.tensor_tensor(msum[:, :], msum[:, :], maskb[:, :], ALU.add).then_inc(msum_ready, 1)
                    if isinstance(i, int) and i == HB - 1:
                        dve.wait_ge(msum_ready, HB)
                        dve.tensor_copy(msum0[:, :], msum[:, :]).then_inc(halved, 1)
                        dve.wait_ge(halved, 1)
                        dve.memset(msum[:, :], 0.0).then_inc(halved, 1)
                        dve.wait_ge(halved, 2)
                    dve.tensor_tensor(pose, pre_ps, regionrow[:, :], ALU.add).then_inc(pose_ready, 1)
                    dve.wait_ge(pose_ready, i + 1)
                    dve.wait_ge(idxf_ready, i + 1)
                    for k in range(TOPK):
                        t = dve.scalar_tensor_tensor(junk[:, k, :], expertno[:, :], idxf[:, k:k + 1], pose, ALU.is_equal,
                                                     ALU.mult, accum_out=posf[:, k:k + 1])
                    t.then_inc(posf_ready, 1)
                    dve.wait_ge(posf_ready, i + 1)
                    dve.tensor_copy(posi[:, s, :], posf).then_inc(pos_ready, 1)

            def normalise_2(i, s):
                if there(i):
                    dve.wait_ge(rstd2_ready, i + 1)
                    dve.wait_ge(dispatched[s], dispatched_count(i, s))
                    dve.tensor_scalar(h2x[:, s, 0, 0:D], X[:, i, :], mv2[:, 0:1], rstd2, ALU.subtract,
                                      ALU.mult).then_inc(h2_ready, 1)
                    dve.wait_ge(h2_ready, i + 1)
                    dve.tensor_copy(h2x[:, s, 1:TOPK, 0:D],
                                    h2x[:, s, 0:1, 0:D].broadcast_to([P, TOPK - 1, D])).then_inc(h2c_ready, 1)

            def add_shared(i):
                if there(i):
                    dve.wait_ge(sd_made, i + 1)
                    dve.tensor_tensor(X[:, i, :], X[:, i, :], sd_ps, ALU.add).then_inc(resid_ready, 1)

            def step(i, s):
                divide(i - 2)
                route(i - 3)
                shared_hidden(i - 3)
                add_attention(i - 2)
                weigh(i - 3, 1 - s)
                place(i - 3, 1 - s)
                normalise_2(i - 2, s)
                add_shared(i - 3)
                stats_1(i + 2, s)
                normalise_1(i + 1, 1 - s)
                row_max(i)

            stats_1(0, 0)
            stats_1(1, 1)
            normalise_1(0, 0)
            steps(dve, step)

            dve.wait_ge(counts_made, 1)
            dve.tensor_tensor(padrow[:, 1, :], ps[0:1, 1, 0:E], regionrow[0:1, :], ALU.add).then_inc(padrow_ready, 1)
            dve.tensor_scalar(cin[:, 0:2], ps[0:E, 0, 0:2], float(P - 1), None, ALU.add).then_inc(tab_step, 1)
            dve.wait_ge(tab_step, 1)
            dve.tensor_copy(cii[:, 0:2], cin[:, 0:2]).then_inc(tab_step, 1)
            dve.wait_ge(tab_step, 2)
            dve.tensor_scalar(cii[:, 2:4], cii[:, 0:2], 7, None, ALU.arith_shift_right).then_inc(tab_step, 1)
            dve.wait_ge(tab_step, 3)
            dve.tensor_copy(colb[:, 0:2], cii[:, 2:4]).then_inc(tab_step, 1)
            dve.wait_ge(tab_step, 4)
            dve.tensor_scalar(colb[:, 2:4], colb[:, 0:2], -1.0, float(REGION), ALU.mult, ALU.add).then_inc(tab_step, 1)
            dve.wait_ge(ends_made, 1)
            dve.wait_ge(tileno_ready, 1)
            dve.tensor_copy(cin[:, 2:4], ps[0:E, 2, 0:2])
            dve.tensor_copy(tilef, tilei).then_inc(tab_step, 1)
            dve.wait_ge(tab_step, 6)
            dve.tensor_scalar(geb[:, 0, :], tilef, cin[:, 2:3], None, ALU.is_ge)
            dve.tensor_scalar(geb[:, 1, :], tilef, cin[:, 3:4], None, ALU.is_ge).then_inc(tab_step, 1)
            dve.wait_ge(rows_made, 1)
            dve.tensor_scalar(etab[:, :], ps[0:1, 3, 0:TILES], float(E - 1), None, ALU.min)
            for h in range(2):
                dve.tensor_tensor(rowf[h], ps[0:1, 4, h * TH:(h + 1) * TH], tilef[0:1, :], ALU.add).then_inc(tab_step, 1)
                dve.wait_ge(tab_step, 8 + h)
                t = dve.tensor_scalar(rtab[:, h * TH:(h + 1) * TH], rowf[h], float(SPARE), None, ALU.min)
            t.then_inc(tab_ready, 1)

            def tile_copy_x(j, u):
                if tile_there(j):
                    dve.wait_ge(xT_made, j + 1)
                    if not (isinstance(j, int) and j < 2):
                        dve.wait_ge(gu_made, j - 1)
                    dve.tensor_copy(xTs[:, u % 2, :, :],
                                    ps[:, u % 2, 0:D].rearrange("p (c t) -> p c t", c=KC)).then_inc(xT_ready, 1)

            def tile_copy_hidden(j, u):
                if tile_there(j):
                    dve.wait_ge(hT_made, j + 1)
                    if not (isinstance(j, int) and j < 2):
                        dve.wait_ge(eo_made, j - 1)
                    dve.tensor_copy(hTs[:, u % 2, :], ps[0:I, 4 + u % 2, 0:P]).then_inc(hT_ready, 1)

            def tile_hidden(j, u):
                if tile_there(j):
                    dve.wait_ge(gate_ready, j + 1)
                    if not (isinstance(j, int) and j < 2):
                        dve.wait_ge(hT_made, j - 1)
                    dve.scalar_tensor_tensor(hid[:, u % 2, :], gate[:, u % 2, :], xt[:, u % NS, D:D + 1],
                                             ps[:, 2 + u % 2, I:2 * I], ALU.mult, ALU.mult).then_inc(hid_ready, 1)

            def tile_step(j, u):
                tile_copy_x(j, u)
                tile_copy_hidden(j - 3, u + 5)
                tile_hidden(j - 1, u + 7)

            tile_steps(dve, tile_step)

            total = PT[:, 0:4, :].rearrange("p (s a) b -> p s (a b)", s=2)
            with dve.Fori(0, NB - (NS - 1), NS) as i:
                for s in range(NS):
                    dve.wait_ge(res_in[s], i * 2 + 16)
                    dve.wait_ge(out_ready, i + max(s - 1, 0))
                    dve.tensor_reduce(total[:, s % 2, :], res[:, s, :, :].rearrange("p k d -> p d k"), AX.X,
                                      ALU.add).then_inc(red_done, 1)
                    dve.wait_ge(red_done, i + (s + 1))
                    dve.tensor_tensor(X[:, i + s, :], X[:, i + s, :], total[:, s % 2, :],
                                      ALU.add).then_inc(out_ready, 1)


_OUTS = [((64, 64, 256), 'float32')]


def kernel(**inputs):
    import numpy as np
    import concourse.bacc as _bacc
    from concourse import mybir as _mybir
    from concourse.bass_utils import run_bass_kernel_spmd as _run

    a = {n: np.asarray(v) for n, v in inputs.items()}
    wkv = a['L0_xattn_Wkv_expand']
    k_of = wkv[0:D].reshape(KC, P // (2 * HD), 2, HD, L)
    wk = np.zeros((KC, 2, P // (2 * HD), 2, HD, L), np.float32)
    for par in range(2):
        wk[:, par, :, par] = k_of[:, :, par]
    wk = wk.reshape(KC * 2, P, L).transpose(2, 0, 1)
    wv = wkv[D:2 * D].reshape(HP, 2, HD, L).transpose(3, 1, 0, 2).reshape(L, 2, P)
    w8 = np.concatenate([a['L0_ffn_shared_gate_w'], a['L0_ffn_shared_expert_gate_w'], a['L0_ffn_shared_up_w'],
                         a['L0_ffn_router_w']], axis=0)
    consts = np.zeros((P, C_WIDTH), np.float32)
    consts[:, C_IDENT:C_IDENT + P] = np.eye(P)
    consts[:, C_UPPER:C_UPPER + P] = np.triu(np.ones((P, P)), 1)
    consts[:, C_CAUSAL:C_CAUSAL + 4 * SEQ] = np.tile(np.triu(np.full((SEQ, SEQ), MASKED), 1), (2, 4))
    consts[:, C_EXPERT:C_EXPERT + E] = np.arange(E)
    consts[:, C_REGION:C_REGION + E] = np.arange(E) * (REGION * P)
    arrays = {
        'x': a['x'],
        'ctxT': a['ctx_512'].reshape(NB, P, L).transpose(0, 2, 1),
        'wq': a['L0_xattn_Wq'].T.reshape(KC, P, D).transpose(1, 0, 2),
        'wk': wk,
        'wv': wv,
        'wo': a['L0_xattn_Wout'].T.reshape(KC, P, D).transpose(1, 0, 2),
        'w8': w8.T.reshape(KC, P, W8).transpose(1, 0, 2),
        'sd': a['L0_ffn_shared_down_w'].T,
        'wgu': a['L0_ffn_gate_up_proj'].transpose(2, 0, 1).reshape(KC, P, E, 2 * I).transpose(1, 0, 2, 3),
        'wd': a['L0_ffn_down_proj'].transpose(2, 0, 1),
        'consts': consts,
    }
    arrays = {f"in_{n}_dram": np.ascontiguousarray(v) for n, v in arrays.items()}
    nc = _bacc.Bacc("TRN2", target_bir_lowering=False, num_devices=1)
    args = [nc.dram_tensor(n, v.shape, _mybir.dt.from_np(v.dtype), kind="ExternalInput").ap()
            for n, v in arrays.items()]
    for i, (shape, dtype) in enumerate(_OUTS):
        args.append(nc.dram_tensor(f"out_{i}_dram", shape, _mybir.dt.from_np(np.dtype(dtype)), kind="ExternalOutput").ap())
    build(nc, *args)
    r = _run(nc, [arrays], core_ids=[0])
    return r.results[0]["out_0_dram"]
```
